# Optimizing a Trainium2 kernel written in Bass

```python
import numpy as np
import jax
import jax.numpy as jnp

def _softmax(x, axis=-1):
    return jax.nn.softmax(x, axis=axis)

def _gelu(x):
    return jax.nn.gelu(x, approximate=True)

def _silu(x):
    return jax.nn.silu(x)

def _sigmoid(x):
    return jax.nn.sigmoid(x)

def _layernorm(x, axis=-1, eps=1e-05):
    m = jnp.mean(x, axis=axis, keepdims=True)
    v = jnp.var(x, axis=axis, keepdims=True)
    return (x - m) / jnp.sqrt(v + eps)

def _scatter_add(tgt, idx, src, axis=0):
    return tgt.at[idx].add(src)

def _segment_sum(src, seg, n):
    return jax.ops.segment_sum(src, seg, n)
kernel_name = 'mk_adaln_ffn_d1_seqx_r4_9f8172'

def setup_inputs(seed: int=0):
    np.random.seed(seed)
    _w = jnp.asarray

    def _rec_inputs():
        import jax
        import jax.numpy as jnp
        _rk = jax.random.key(seed)
        x = -0.0003929 + 0.9999 * jax.random.normal(jax.random.fold_in(_rk, 1), (64, 64, 1024), jnp.float32)
        _lenS = 64 - jax.random.randint(jax.random.fold_in(_rk, 7), (64,), 0, max(1, 64 // 4) + 1, jnp.int32)
        _lenS2 = 64 - jax.random.randint(jax.random.fold_in(_rk, 8), (64,), 0, max(1, 64 // 4) + 1, jnp.int32)
        itok_B_8_3872 = jax.random.randint(jax.random.fold_in(_rk, 11), (64,), 8, 3873, jnp.int32)
        return (x, itok_B_8_3872)
    x, itok_B_8_3872 = _rec_inputs()

    def _L0_cond_setup():
        import math
        import jax, jax.numpy as jnp
        import numpy as np
        H, N, B, L = (64, 64, 16, 1024)
        DT_MIN, DT_MAX = (0.001, 0.1)

        def _get_kernel(log_dt, C, log_A_real, A_imag, length):
            Cc = C[..., 0] + 1j * C[..., 1]
            dt = jnp.exp(log_dt)
            A = -jnp.exp(log_A_real) + 1j * A_imag
            dtA = A * dt[:, None]
            P = dtA[:, :, None] * jnp.arange(length, dtype=jnp.float32)
            Cs = Cc * (jnp.exp(dtA) - 1.0) / A
            K = 2.0 * jnp.einsum('hn,hnl->hl', Cs, jnp.exp(P)).real
            return K
        key = jax.random.key(seed)
        ks = jax.random.split(key, 6)
        u = jax.random.normal(ks[0], (B, H, L), dtype=jnp.float32)
        length = jax.random.randint(ks[1], (B,), 0, L)
        log_dt = jax.random.uniform(ks[2], (H,), dtype=jnp.float32) * (math.log(DT_MAX) - math.log(DT_MIN)) + math.log(DT_MIN)
        C = jax.random.normal(ks[3], (H, N, 2), dtype=jnp.float32)
        log_A_real = jnp.log(0.5 * jnp.ones((H, N), dtype=jnp.float32))
        A_imag = math.pi * jnp.broadcast_to(jnp.arange(N, dtype=jnp.float32), (H, N))
        D = jax.random.normal(ks[4], (H,), dtype=jnp.float32)
        return {'u': u, 'length': length, 'log_dt': log_dt, 'C': C, 'log_A_real': log_A_real, 'A_imag': A_imag, 'D': D}
    _L0_cond_all = _L0_cond_setup()
    _L0_cond_in = {k: v for k, v in _L0_cond_all.items() if k in ('log_dt', 'C', 'log_A_real', 'A_imag', 'D')}
    del _L0_cond_all

    def _L0_ffn_setup():
        import jax, jax.numpy as jnp
        import numpy as np
        BATCH, SEQ, D = (2, 512, 1024)
        K, TOPK, RANK = (64, 16, 16)
        ALPHA = 32.0
        SCALING = ALPHA / RANK
        key = jax.random.key(seed)
        k1, k2, k3, k4 = jax.random.split(key, 4)
        x = jax.random.normal(k1, (BATCH, SEQ, D), dtype=jnp.float32)
        A = jax.random.normal(k2, (K, RANK, D), dtype=jnp.float32) * 0.02
        B = jax.random.normal(k3, (K, D, RANK), dtype=jnp.float32) * 0.02
        Wr = jax.random.normal(k4, (K, D), dtype=jnp.float32) * 0.02
        return {'x': x, 'A': A, 'B': B, 'Wr': Wr}
    _L0_ffn_all = _L0_ffn_setup()
    _L0_ffn_in = {k: v for k, v in _L0_ffn_all.items() if k in ('A', 'B', 'Wr')}
    del _L0_ffn_all
    return {'x': x, 'itok_B_8_3872': itok_B_8_3872, 'L0_cond_log_dt': _L0_cond_in['log_dt'], 'L0_cond_C': _L0_cond_in['C'], 'L0_cond_log_A_real': _L0_cond_in['log_A_real'], 'L0_cond_A_imag': _L0_cond_in['A_imag'], 'L0_cond_D': _L0_cond_in['D'], 'L0_ffn_A': _L0_ffn_in['A'], 'L0_ffn_B': _L0_ffn_in['B'], 'L0_ffn_Wr': _L0_ffn_in['Wr']}

def reference(x, itok_B_8_3872, L0_cond_log_dt, L0_cond_C, L0_cond_log_A_real, L0_cond_A_imag, L0_cond_D, L0_ffn_A, L0_ffn_B, L0_ffn_Wr):
    import jax
    import jax.numpy as jnp

    def _L0_cond_ref(u, length, log_dt, C, log_A_real, A_imag, D):
        import math
        import jax, jax.numpy as jnp
        import numpy as np
        H, N, B, L = (64, 64, 16, 1024)
        DT_MIN, DT_MAX = (0.001, 0.1)

        def _get_kernel(log_dt, C, log_A_real, A_imag, length):
            Cc = C[..., 0] + 1j * C[..., 1]
            dt = jnp.exp(log_dt)
            A = -jnp.exp(log_A_real) + 1j * A_imag
            dtA = A * dt[:, None]
            P = dtA[:, :, None] * jnp.arange(length, dtype=jnp.float32)
            Cs = Cc * (jnp.exp(dtA) - 1.0) / A
            K = 2.0 * jnp.einsum('hn,hnl->hl', Cs, jnp.exp(P)).real
            return K
        Bq, Hq, Lq = u.shape
        mask = (jnp.arange(Lq) < length[:, None]).astype(u.dtype)
        u_m = u * mask[:, None, :]
        kernel = _get_kernel(log_dt, C, log_A_real, A_imag, Lq)
        n = 2 * Lq
        k_f = jnp.fft.rfft(kernel, n=n)
        u_f = jnp.fft.rfft(u_m, n=n)
        y = jnp.fft.irfft(u_f * k_f, n=n)[..., :Lq]
        y = y + u_m * D[:, None]
        return y * mask[:, None, :]

    def _L0_ffn_ref(x, A, B, Wr):
        import jax, jax.numpy as jnp
        import numpy as np
        BATCH, SEQ, D = (2, 512, 1024)
        K, TOPK, RANK = (64, 16, 16)
        ALPHA = 32.0
        SCALING = ALPHA / RANK
        prefix = x.shape[:-1]
        xf = x.reshape(-1, x.shape[-1])
        N = xf.shape[0]
        scores = xf @ Wr.T
        top_vals, top_idx = jax.lax.top_k(scores, TOPK)
        gates = jax.nn.softmax(top_vals, axis=-1)
        G = jnp.zeros((N, K), xf.dtype).at[jnp.arange(N)[:, None], top_idx].set(gates)
        h = jnp.einsum('nd,krd->nkr', xf, A)
        out = jnp.einsum('nkr,kdr->nd', h * G[:, :, None], B)
        return (out * SCALING).reshape(*prefix, -1)
    x = x + _L0_ffn_ref(_L0_cond_ref(x, itok_B_8_3872, L0_cond_log_dt, L0_cond_C, L0_cond_log_A_real, L0_cond_A_imag, L0_cond_D), L0_ffn_A, L0_ffn_B, L0_ffn_Wr)
    return x

_drawn_inputs = setup_inputs


def setup_inputs(seed=0):
    import zlib

    import numpy as np

    out = dict(_drawn_inputs(seed))
    spreads = {'L0_cond_log_A_real': (-0.6931471824645996, 0.2)}
    factors = {}
    for name, (base, spread) in spreads.items():
        noise = np.random.default_rng([zlib.crc32(name.encode()), seed]).standard_normal(out[name].shape)
        drawn = base * np.exp(spread * noise) if base else spread * noise
        out[name] = jnp.asarray(drawn.astype(out[name].dtype))
    for name, factor in factors.items():
        out[name] = (out[name] * factor).astype(out[name].dtype)
    return out
```

```python
from contextlib import ExitStack

import concourse.bass as bass
from concourse import mybir

P = 128
B, H, L = 64, 64, 1024
N = 64
E, R = 64, 16
D = L
ER = E * R
HT = P // B
TILES = H // HT
NC = L // P
NE = ER // P
EW = ER + E
HALF = 512
TOPK = 16
SCALING = 32.0 / 16
GRID = 32
HC = 8
CHUNKS = H // HC
PAD = P - 1
KROW = 1152
STAGES = 3
NEG = -3.0e38

F32 = mybir.dt.float32
F32R = mybir.dt.float32r
I32 = mybir.dt.int32
BF16 = mybir.dt.bfloat16
ALU = mybir.AluOpType
ACT = mybir.ActivationFunctionType

ROUND = 12582912.0
LOG2E = 1.4426950408889634
LN2_HI, LN2_LO = 0.693359375, -2.12194440e-4
INV_2PI = 0.15915494309189535
TWO_PI_1, TWO_PI_2, TWO_PI_3 = 6.28125, 0.0019350051879882812, 3.0199159819e-07
TWO_PI, PI = 6.2831850, 3.1415925


def build(nc, xt, x, length, parameters, a_t, b_t, wr_t, out):
    k_dram = nc.dram_tensor("k_padded", (H, KROW), F32, kind="Internal")
    k_ap = k_dram.ap()

    def toeplitz(t, i):
        return bass.AP(k_dram, t * (HT * KROW) + i * KROW, [[1, P], [1, L]])

    def rows(array, t):
        return bass.AP(array.tensor, t * (HT * L), [[L, HT], [H * L, B], [1, L]])

    with ExitStack() as ctx:
        def sb(name, shape, dt=F32, where=ctx):
            return where.enter_context(nc.sbuf_tensor(name, shape, dt))

        def ps(name, shape):
            return ctx.enter_context(nc.psum_tensor(name, shape, F32))

        def sem(name):
            return ctx.enter_context(nc.semaphore(name))

        a_hi, a_lo = sb("a_hi", [P, NC, EW], F32R), sb("a_lo", [P, NC, EW], F32R)
        t_hi, t_lo = sb("t_hi", [P, HT, L], F32R), sb("t_lo", [P, HT, L], F32R)
        xt_in = sb("xt_in", [P, HT, NC * B])
        xt_hi, xt_lo = sb("xt_hi", [P, HT, NC * B], F32R), sb("xt_lo", [P, HT, NC * B], F32R)
        y_m = sb("y_m", [P, NC, P])
        y_hi, y_lo = sb("y_hi", [P, NC, P], F32R), sb("y_lo", [P, NC, P], F32R)
        g_hi, g_lo = sb("g_hi", [P, NE, P], F32R), sb("g_lo", [P, NE, P], F32R)
        x_in = sb("x_in", [P, D])
        wide = sb("wide", [P, D])
        hg = o_sb = wide
        mask = sb("mask", [P, NC, B], BF16)
        ident = sb("ident", [P, P])
        stage = sb("stage", [P, STAGES, ER])
        top_a, top_b = sb("top_a", [P, 8]), sb("top_b", [P, 8])
        score_sb = sb("score_sb", [P, E])
        rest_a, rest_b = sb("rest_a", [P, E]), sb("rest_b", [P, E])
        neg_max, gate_sum, gate_scale = sb("neg_max", [P, 1]), sb("gate_sum", [P, 2]), sb("gate_scale", [P, 1])
        exp_all, exp_rest, gates = sb("exp_all", [P, E]), sb("exp_rest", [P, E]), sb("gates", [P, E])
        rates, turns = sb("rates", [P, 2, H]), sb("turns", [P, 2, H])
        alpha, beta = sb("alpha", [P, H]), sb("beta", [P, H])
        grid, phase, skip = sb("grid", [P, GRID]), sb("phase", [P, 1]), sb("skip", [1, H])

        with ExitStack() as early:
            def scratch(name, shape, dt=F32):
                return sb(name, shape, dt, early)

            par = scratch("par", [P, 6, H])
            len_i, len_f = scratch("len_i", [P, B], I32), scratch("len_f", [P, B])
            pos_i, pos_f = scratch("pos_i", [P, NC], I32), scratch("pos_f", [P, NC])
            grid_i = scratch("grid_i", [P, GRID], I32)
            zeros = scratch("zeros", [H, PAD])
            tmp = [scratch(f"tmp{i}", [P, 2, H]) for i in range(6)]
            pow_i = scratch("pow_i", [P, 2, H], I32)
            sin_half, sin_full = scratch("sin_half", [P, H]), scratch("sin_full", [P, H])
            er, ei, fr, fi = (scratch(n, [P, H]) for n in ("er", "ei", "fr", "fi"))
            chunk0 = scratch("chunk0", [P, 11 * HC * GRID])
        logs, aim, cc = par[:, 0:2, :], par[:, 2, :], par[:, 3:5, :]
        b_hi, b_lo = sb("b_hi", [P, NE, D], F32R), sb("b_lo", [P, NE, D], F32R)

        def chunk_views(flat):
            def part(first, n, rows=P):
                v = flat[0:rows, first * HC * GRID:(first + n) * HC * GRID]
                return v.rearrange("p (j h g) -> p j h g", j=n, g=GRID)
            return part(0, 2), part(2, 3), part(5, 3), part(8, 2), part(10, 1, GRID)

        views0 = chunk_views(chunk0[:, :])
        views = chunk_views(stage[:, :, :].rearrange("p s n -> p (s n)"))

        conv_ps = [ps(f"conv_ps{i}", [P, NC * B]) for i in range(HT)]
        h_ps = ps("h_ps", [P, 2, HALF])
        turn_ps = ps("turn_ps", [P, 2, HALF])
        out_ps = ps("out_ps", [P, 2, HALF])
        H_PARTS = [(h_ps[:, 0, 0:384], 0, 384, 384), (h_ps[:, 1, 0:384], 384, 384, 384),
                   (turn_ps[:, 0, 0:EW - 768], 768, EW - 768, ER - 768)]
        scores = turn_ps[:, 0, ER - 768:EW - 768]
        k_ps = turn_ps[0:GRID, 1, 0:HC * GRID]

        s_par, s_len, s_zero, s_xt, s_x, s_out, s_k = (
            sem(n) for n in ("s_par", "s_len", "s_zero", "s_xt", "s_x", "s_out", "s_k"))
        s_t = [sem(f"s_t{i}") for i in range(HT)]
        s_w = [sem(f"s_w{i}") for i in range(STAGES)]
        s_iota, s_ident, s_calc, s_zeroed = sem("s_iota"), sem("s_ident"), sem("s_calc"), sem("s_zeroed")
        s_mask, s_turns, s_sins, s_whi, s_wlo = sem("s_mask"), sem("s_turns"), sem("s_sins"), sem("s_whi"), sem("s_wlo")
        s_theta, s_whole, s_angle, s_wave, s_mixed, s_factors, s_kps, s_kcopy, s_kdone = (
            sem(n) for n in ("s_theta", "s_whole", "s_angle", "s_wave", "s_mixed", "s_factors", "s_kps", "s_kcopy", "s_kdone"))
        s_thi, s_tlo, s_xhi, s_xlo = sem("s_thi"), sem("s_tlo"), sem("s_xhi"), sem("s_xlo")
        s_conv, s_ym, s_yhi, s_ylo = sem("s_conv"), sem("s_ym"), sem("s_yhi"), sem("s_ylo")
        s_router, s_negmax, s_rest, s_exp, s_passed, s_scale = (
            sem(n) for n in ("s_router", "s_negmax", "s_rest", "s_exp", "s_passed", "s_scale"))
        s_up, s_hg, s_turn, s_ghi, s_glo, s_down, s_o = (sem(n) for n in ("s_up", "s_hg", "s_turn", "s_ghi", "s_glo", "s_down", "s_o"))

        def staged(i, n=ER):
            return stage[:, i % STAGES, 0:n]

        loads = [(wr_t, staged(0, NC * E).rearrange("p (c e) -> p c e", e=E), a_hi[:, :, ER:EW], a_lo[:, :, ER:EW])]
        loads += [(a_t[:, c, :], staged(1 + c), a_hi[:, c, 0:ER], a_lo[:, c, 0:ER]) for c in range(NC)]
        FIRST_B = len(loads)
        loads += [(b_t[:, c, :], staged(FIRST_B + c), b_hi[:, c, :], b_lo[:, c, :]) for c in range(NE)]

        block = ctx.enter_context(nc.Block())

        @block.sync
        def _(sp):
            def load_weights(i):
                if i >= STAGES:
                    sp.wait_ge(s_wlo, i - STAGES + 1)
                src, dst, _, _ = loads[i]
                sp.dma_start(dst, src).then_inc(s_w[i % STAGES], 16)

            def load_toeplitz(t, i):
                sp.dma_start(t_lo[:, i, :].bitcast(F32), toeplitz(t, i)).then_inc(s_t[i], 16)

            def store_k(c, view):
                dst = bass.AP(k_dram, c * (HC * KROW) + PAD, [[GRID, GRID], [KROW, HC], [1, GRID]])
                sp.dma_start(dst, view[:, 0]).then_inc(s_k, 16)

            sp.dma_start(par[:, :, :], parameters).then_inc(s_par, 16)
            load_weights(0)
            sp.dma_start(xt_in[:, :, :], xt[0, :, :]).then_inc(s_xt, 16)
            for i in range(1, STAGES):
                load_weights(i)
            sp.dma_start(len_i[:, :], length.partition_broadcast(P)).then_inc(s_len, 16)
            sp.wait_ge(s_zeroed, 1)
            sp.dma_start(k_ap[:, 0:PAD], zeros[:, :]).then_inc(s_zero, 16)
            sp.dma_start(x_in[:, :], rows(x, 0)).then_inc(s_x, 16)
            for i in range(STAGES, FIRST_B):
                load_weights(i)
            sp.wait_ge(s_kdone, 1)
            store_k(0, views0[4])
            sp.wait_ge(s_zero, 16)
            sp.wait_ge(s_k, 16)
            for i in range(HT):
                load_toeplitz(0, i)
            for i in range(FIRST_B, FIRST_B + STAGES):
                load_weights(i)
            sp.wait_ge(s_xlo, 1)
            sp.dma_start(xt_in[:, :, :], xt[1, :, :]).then_inc(s_xt, 16)
            for i in range(FIRST_B + STAGES, len(loads) - 2):
                load_weights(i)
            for i in range(HT):
                sp.wait_ge(s_conv, i + 1)
                load_toeplitz(1, i)
            for i in range(len(loads) - 2, len(loads)):
                load_weights(i)

            def step(t, ahead2=True, ahead1=True, chunk=False, chunks_done=False):
                if ahead2:
                    sp.wait_ge(s_xlo, t + 2)
                    sp.dma_start(xt_in[:, :, :], xt[bass.ds(t + 2, 1), :, :].rearrange("t p n -> (t p) n")).then_inc(s_xt, 16)
                    if chunk:
                        sp.wait_ge(s_k, 16 * t)
                    if chunks_done:
                        sp.wait_ge(s_k, 16 * CHUNKS)
                    for i in range(HT):
                        sp.wait_ge(s_conv, HT * t + HT + i + 1)
                        load_toeplitz(t + 2, i)
                sp.wait_ge(s_o, t + 1)
                sp.dma_start(rows(out, t), o_sb[:, :]).then_inc(s_out, 16)
                if ahead1:
                    sp.dma_start(x_in[:, :], rows(x, t + 1)).then_inc(s_x, 16)
                if chunk:
                    sp.wait_ge(s_kdone, t + 1)
                    store_k(t, views[4])

            step(0)
            with sp.Fori(1, CHUNKS) as t:
                step(t, chunk=True)
            with sp.Fori(CHUNKS, TILES - 2) as t:
                step(t, chunks_done=True)
            step(TILES - 2, ahead2=False)
            step(TILES - 1, ahead2=False, ahead1=False)
            sp.wait_ge(s_out, 16 * TILES)

        @block.gpsimd
        def _(pool):
            pool.iota(grid_i[:, :], pattern=[[1, GRID]], base=0, channel_multiplier=0).then_inc(s_iota, 1)
            pool.iota(pos_i[:, :], pattern=[[P, NC]], base=0, channel_multiplier=1).then_inc(s_iota, 1)
            pool.memset(zeros[:, :], 0.0).then_inc(s_zeroed, 1)
            pool.memset(ident[:, :], 0.0).then_inc(s_ident, 1)
            pool.wait_ge(s_ident, 1)
            pool.affine_select(out=ident[:, :], in_=ident[:, :], compare_op=ALU.not_equal, fill=1.0,
                               base=0, pattern=[[-1, P]], channel_multiplier=1).then_inc(s_ident, 1)
            for i, (_, staged_w, hi, lo) in enumerate(loads):
                pool.wait_ge(s_whi, i + 1)
                pool.tensor_tensor(out=lo, in0=staged_w, in1=hi.bitcast(F32), op=ALU.subtract).then_inc(s_wlo, 1)

        @block.scalar
        def _(act):
            def split_weights(i):
                if i == FIRST_B:
                    act.wait_ge(s_k, 16)
                    act.wait_ge(s_zero, 16)
                    act.wait_ge(s_mask, 1)
                act.wait_ge(s_w[i % STAGES], 16 * (i // STAGES + 1))
                _, staged_w, hi, _ = loads[i]
                act.activation(hi, staged_w, ACT.Copy).then_inc(s_whi, 1)

            def waves(c, buffers):
                _, _, wave, decay, _ = buffers
                act.wait_ge(s_angle, c + 1)
                act.activation(wave, wave, ACT.Sin, scale=TWO_PI).then_inc(s_wave, 1)
                act.activation(decay, decay, ACT.Exp).then_inc(s_wave, 1)

            def copy_k(c, buffers):
                act.wait_ge(s_kps, c + 1)
                act.activation(buffers[4][:, 0].rearrange("a h b -> a (h b)"), k_ps, ACT.Copy).then_inc(s_kcopy, 1)

            def high_t(t, i):
                act.wait_ge(s_t[i], 16 * t + 16)
                act.activation(t_hi[:, i, :], t_lo[:, i, :].bitcast(F32), ACT.Copy).then_inc(s_thi, 1)

            def high_y(t):
                act.wait_ge(s_ym, HT * t + HT)
                act.activation(y_hi[:, :, :], y_m[:, :, :], ACT.Copy).then_inc(s_yhi, 1)

            split_weights(0)
            act.wait_ge(s_xt, 16)
            act.activation(xt_hi[:, :, :], xt_in[:, :, :], ACT.Copy).then_inc(s_xhi, 1)
            split_weights(1)
            split_weights(2)
            act.wait_ge(s_turns, 1)
            act.activation(sin_half[:, :], turns[:, 0, :], ACT.Sin, scale=PI).then_inc(s_sins, 1)
            act.activation(sin_full[:, :], turns[:, 0, :], ACT.Sin, scale=TWO_PI).then_inc(s_sins, 1)
            waves(0, views0)
            for i in range(3, FIRST_B - 2):
                split_weights(i)
            copy_k(0, views0)
            for i in range(FIRST_B - 2, FIRST_B):
                split_weights(i)
            high_t(0, 0)
            high_t(0, 1)
            high_y(0)
            for i in range(FIRST_B, len(loads)):
                split_weights(i)

            def step(t, ahead=True, chunk=False):
                if ahead:
                    act.wait_ge(s_conv, HT * t + HT)
                    act.wait_ge(s_xt, 16 * t + 32)
                    act.activation(xt_hi[:, :, :], xt_in[:, :, :], ACT.Copy).then_inc(s_xhi, 1)
                    for i in range(HT):
                        high_t(t + 1, i)
                act.wait_ge(s_negmax, t + 1)
                act.activation(exp_all[:, :], score_sb[:, :], ACT.Exp, bias=neg_max[:, :]).then_inc(s_exp, 1)
                act.wait_ge(s_rest, t + 1)
                act.activation(exp_rest[:, :], rest_b[:, :], ACT.Exp, bias=neg_max[:, :]).then_inc(s_exp, 1)
                for n, bank in enumerate((1, 0)):
                    act.wait_ge(s_turn, 2 * t + n + 1)
                    act.activation(g_hi[:, 4 * bank:4 * bank + 4, :].rearrange("p c n -> p (c n)"), turn_ps[:, bank, :],
                                   ACT.Copy).then_inc(s_ghi, 1)
                if ahead:
                    high_y(t + 1)
                if chunk:
                    waves(t, views)
                    act.wait_ge(s_k, 16 * t)
                    copy_k(t, views)

            step(0)
            with act.Fori(1, CHUNKS) as t:
                step(t, chunk=True)
            with act.Fori(CHUNKS, TILES - 1) as t:
                step(t)
            step(TILES - 1, ahead=False)

        @block.vector
        def _(dve):
            calc = [0]

            def link(ins):
                calc[0] += 1
                ins.then_inc(s_calc, 1)
                dve.wait_ge(s_calc, calc[0])

            def exp_parts(v):
                k, r, q = (tmp[i][:, :, :] for i in range(3))
                link(dve.tensor_scalar(r, v, -87.0, 88.0, ALU.max, ALU.min))
                link(dve.tensor_scalar(k, r, LOG2E, ROUND, ALU.mult, ALU.add))
                link(dve.tensor_scalar(k, k, ROUND, None, ALU.subtract))
                link(dve.scalar_tensor_tensor(out=r, in0=k, scalar=-LN2_HI, in1=r, op0=ALU.mult, op1=ALU.add))
                link(dve.scalar_tensor_tensor(out=r, in0=k, scalar=-LN2_LO, in1=r, op0=ALU.mult, op1=ALU.add))
                dve.tensor_scalar(pow_i[:, :, :], k, 8388608.0, 127.0 * 8388608.0, ALU.mult, ALU.add)
                link(dve.tensor_scalar(q, r, 1.0 / 5040, 1.0 / 720, ALU.mult, ALU.add))
                link(dve.tensor_tensor(out=q, in0=q, in1=r, op=ALU.mult))
                for coefficient in (1.0 / 120, 1.0 / 24, 1.0 / 6, 0.5, 1.0):
                    link(dve.scalar_tensor_tensor(out=q, in0=q, scalar=coefficient, in1=r, op0=ALU.add, op1=ALU.mult))
                return pow_i[:, :, :].bitcast(F32), q

            def angles(c, buffers):
                theta, whole, wave, decay, _ = buffers
                heads = bass.ds(c * HC, HC)
                full = [P, 2, HC, GRID]
                g_b = grid[:, :].unsqueeze(1).unsqueeze(1).to_broadcast(full)
                dve.tensor_tensor(out=theta, in0=turns[:, :, heads].unsqueeze(3).to_broadcast(full), in1=g_b,
                                  op=ALU.mult).then_inc(s_theta, 1)
                dve.tensor_tensor(out=decay, in0=rates[:, :, heads].unsqueeze(3).to_broadcast(full), in1=g_b, op=ALU.mult)
                dve.wait_ge(s_theta, c + 1)
                dve.tensor_scalar(wave[:, 0], theta[:, 0], phase[:, :], None, ALU.add)
                dve.tensor_scalar(wave[:, 1], theta[:, 1], 0.25, None, ALU.add)
                dve.tensor_scalar(whole[:, 2], theta[:, 1], ROUND, ROUND, ALU.add, ALU.subtract).then_inc(s_whole, 1)
                dve.wait_ge(s_whole, 2 * c + 1)
                dve.tensor_scalar(whole[:, 0:2], wave[:, 0:2], ROUND, ROUND, ALU.add, ALU.subtract).then_inc(s_whole, 1)
                dve.tensor_tensor(out=wave[:, 2], in0=theta[:, 1], in1=whole[:, 2], op=ALU.subtract)
                dve.wait_ge(s_whole, 2 * c + 2)
                dve.tensor_tensor(out=wave[:, 0:2], in0=wave[:, 0:2], in1=whole[:, 0:2], op=ALU.subtract).then_inc(s_angle, 1)

            def factors(c, buffers):
                _, _, wave, decay, _ = buffers
                heads = bass.ds(c * HC, HC)
                dve.wait_ge(s_wave, 2 * c + 2)
                al = alpha[:, heads].unsqueeze(2).to_broadcast([P, HC, GRID])
                be = beta[:, heads].unsqueeze(2).to_broadcast([P, HC, GRID])
                dve.tensor_tensor(out=wave[:, 1], in0=wave[:, 1], in1=al, op=ALU.mult)
                dve.tensor_tensor(out=wave[:, 2], in0=wave[:, 2], in1=be, op=ALU.mult).then_inc(s_mixed, 1)
                dve.tensor_tensor(out=wave[:, 0], in0=wave[:, 0], in1=decay[:, 0], op=ALU.mult)
                dve.wait_ge(s_mixed, 2 * c + 1)
                dve.tensor_tensor(out=wave[:, 1], in0=wave[:, 1], in1=wave[:, 2], op=ALU.add).then_inc(s_mixed, 1)
                dve.wait_ge(s_mixed, 2 * c + 2)
                dve.tensor_tensor(out=wave[:, 1], in0=wave[:, 1], in1=decay[:, 1], op=ALU.mult).then_inc(s_factors, 1)

            def add_skip(c, buffers):
                heads = bass.ds(c * HC, HC)
                dve.wait_ge(s_kcopy, c + 1)
                first = buffers[4][0:1, 0, :, 0]
                dve.tensor_tensor(out=first, in0=first, in1=skip[:, heads], op=ALU.add).then_inc(s_kdone, 1)

            def low_t(t, i):
                dve.wait_ge(s_thi, HT * t + i + 1)
                dve.tensor_tensor(out=t_lo[:, i, :], in0=t_lo[:, i, :].bitcast(F32), in1=t_hi[:, i, :].bitcast(F32),
                                  op=ALU.subtract).then_inc(s_tlo, 1)

            def low_x(t):
                dve.wait_ge(s_xhi, t + 1)
                dve.tensor_tensor(out=xt_lo[:, :, :], in0=xt_in[:, :, :], in1=xt_hi[:, :, :].bitcast(F32),
                                  op=ALU.subtract).then_inc(s_xlo, 1)

            def mask_y(t, i):
                dve.wait_ge(s_conv, HT * t + i + 1)
                dve.tensor_tensor(out=y_m[:, :, i * B:(i + 1) * B], in0=conv_ps[i][:, :].rearrange("p (c b) -> p c b", b=B),
                                  in1=mask[:, :, :], op=ALU.mult).then_inc(s_ym, 1)

            def low_y(t):
                dve.wait_ge(s_yhi, t + 1)
                dve.tensor_tensor(out=y_lo[:, :, :], in0=y_m[:, :, :], in1=y_hi[:, :, :].bitcast(F32), op=ALU.subtract).then_inc(s_ylo, 1)

            dve.memset(phase[0:N, :], 0.25)
            dve.memset(phase[N:P, :], 0.0)
            dve.wait_ge(s_iota, 2)
            dve.tensor_copy(pos_f[:, :], pos_i[:, :])
            dve.tensor_copy(grid[:, :], grid_i[:, :])
            dve.wait_ge(s_par, 16)
            dve.tensor_copy(skip[:, :], par[0:1, 5, :])

            s, q = exp_parts(logs)
            dt_a = tmp[4]
            link(dve.scalar_tensor_tensor(out=dt_a[:, :, :], in0=q, scalar=1.0, in1=s, op0=ALU.add, op1=ALU.mult))
            dt, a = dt_a[:, 0, :], dt_a[:, 1, :]
            im, kk = tmp[5][:, 0, :], tmp[5][:, 1, :]
            dve.scalar_tensor_tensor(out=rates[:, 0, :], in0=a, scalar=-1.0, in1=dt, op0=ALU.mult, op1=ALU.mult)
            link(dve.tensor_tensor(out=im, in0=aim, in1=dt, op=ALU.mult))
            link(dve.tensor_scalar(kk, im, INV_2PI, ROUND, ALU.mult, ALU.add))
            link(dve.tensor_scalar(kk, kk, ROUND, None, ALU.subtract))
            for part in (TWO_PI_1, TWO_PI_2, TWO_PI_3):
                link(dve.scalar_tensor_tensor(out=im, in0=kk, scalar=-part, in1=im, op0=ALU.mult, op1=ALU.add))
            dve.tensor_scalar(turns[:, 0, :], im, INV_2PI, None, ALU.mult).then_inc(s_turns, 1)
            dve.tensor_scalar(rates[:, 1, :], rates[:, 0, :], float(GRID), None, ALU.mult)
            dve.wait_ge(s_turns, 1)
            link(dve.tensor_scalar(im, turns[:, 0, :], float(GRID), None, ALU.mult))
            link(dve.tensor_scalar(kk, im, ROUND, ROUND, ALU.add, ALU.subtract))
            link(dve.tensor_tensor(out=turns[:, 1, :], in0=im, in1=kk, op=ALU.subtract))
            angles(0, views0)

            em1 = tmp[2]
            s, q = exp_parts(rates[:, :, :])
            link(dve.tensor_tensor(out=em1[:, :, :], in0=q, in1=s, op=ALU.mult))
            link(dve.scalar_tensor_tensor(out=em1[:, :, :], in0=s, scalar=-1.0, in1=em1[:, :, :], op0=ALU.add, op1=ALU.add))
            em1 = em1[:, 0, :]
            dve.wait_ge(s_sins, 2)
            cm1, den = tmp[0][:, 0, :], tmp[1][:, 0, :]
            u, v = tmp[0][:, 1, :], tmp[1][:, 1, :]
            dve.tensor_tensor(out=u, in0=a, in1=a, op=ALU.mult)
            dve.tensor_tensor(out=v, in0=aim, in1=aim, op=ALU.mult)
            link(dve.scalar_tensor_tensor(out=cm1, in0=sin_half[:, :], scalar=-2.0, in1=sin_half[:, :], op0=ALU.mult, op1=ALU.mult))
            dve.scalar_tensor_tensor(out=ei[:, :], in0=em1, scalar=1.0, in1=sin_full[:, :], op0=ALU.add, op1=ALU.mult)
            dve.tensor_tensor(out=den, in0=u, in1=v, op=ALU.add)
            link(dve.scalar_tensor_tensor(out=er[:, :], in0=cm1, scalar=1.0, in1=em1, op0=ALU.add, op1=ALU.mult))
            dve.reciprocal(den, den)
            link(dve.tensor_tensor(out=er[:, :], in0=er[:, :], in1=cm1, op=ALU.add))
            dve.tensor_tensor(out=u, in0=a, in1=er[:, :], op=ALU.mult)
            link(dve.tensor_tensor(out=v, in0=aim, in1=ei[:, :], op=ALU.mult))
            link(dve.tensor_tensor(out=fr[:, :], in0=v, in1=u, op=ALU.subtract))
            dve.tensor_tensor(out=u, in0=a, in1=ei[:, :], op=ALU.mult)
            link(dve.tensor_tensor(out=v, in0=aim, in1=er[:, :], op=ALU.mult))
            link(dve.scalar_tensor_tensor(out=fi[:, :], in0=u, scalar=-1.0, in1=v, op0=ALU.mult, op1=ALU.subtract))
            dve.tensor_tensor(out=fr[:, :], in0=fr[:, :], in1=den, op=ALU.mult)
            link(dve.tensor_tensor(out=fi[:, :], in0=fi[:, :], in1=den, op=ALU.mult))
            c_re, c_im = cc[:, 0, :], cc[:, 1, :]
            dve.tensor_tensor(out=tmp[0][:, 0, :], in0=c_re, in1=fr[:, :], op=ALU.mult)
            dve.tensor_tensor(out=tmp[0][:, 1, :], in0=c_im, in1=fi[:, :], op=ALU.mult)
            dve.tensor_tensor(out=tmp[1][:, 0, :], in0=c_re, in1=fi[:, :], op=ALU.mult)
            link(dve.tensor_tensor(out=tmp[1][:, 1, :], in0=c_im, in1=fr[:, :], op=ALU.mult))
            dve.tensor_tensor(out=er[:, :], in0=tmp[0][:, 0, :], in1=tmp[0][:, 1, :], op=ALU.subtract)
            link(dve.tensor_tensor(out=ei[:, :], in0=tmp[1][:, 0, :], in1=tmp[1][:, 1, :], op=ALU.add))
            dve.tensor_scalar(alpha[0:N, :], er[0:N, :], 2.0, None, ALU.mult)
            dve.tensor_scalar(alpha[N:P, :], ei[N:P, :], -2.0, None, ALU.mult)
            dve.tensor_scalar(beta[0:N, :], ei[0:N, :], -2.0, None, ALU.mult)
            link(dve.tensor_scalar(beta[N:P, :], er[N:P, :], -2.0, None, ALU.mult))
            factors(0, views0)
            low_x(0)
            add_skip(0, views0)
            dve.wait_ge(s_len, 16)
            link(dve.tensor_copy(len_f[:, :], len_i[:, :]))
            dve.tensor_tensor(out=mask[:, :, :], in0=pos_f[:, :].unsqueeze(2).to_broadcast([P, NC, B]),
                              in1=len_f[:, :].unsqueeze(1).to_broadcast([P, NC, B]), op=ALU.is_lt).then_inc(s_mask, 1)
            for i in range(HT):
                low_t(0, i)
            for i in range(HT):
                mask_y(0, i)
            low_y(0)

            def step(t, ahead=True, first=False, chunk=False):
                if ahead:
                    low_x(t + 1)
                    for i in range(HT):
                        low_t(t + 1, i)
                if chunk:
                    dve.wait_ge(s_wlo, len(loads))
                    dve.wait_ge(s_kps, t)
                    angles(t, views)
                dve.wait_ge(s_up, t + 1)
                dve.tensor_copy(score_sb[:, :], scores).then_inc(s_router, 1)
                dve.max(out=top_a[:, :], in_=scores).then_inc(s_router, 1)
                dve.wait_ge(s_router, 6 * t + 2)
                dve.tensor_scalar(neg_max[:, :], top_a[:, 0:1], -1.0, None, ALU.mult).then_inc(s_negmax, 1)
                dve.match_replace(out=rest_a[:, :], in_to_replace=top_a[:, :], in_values=score_sb[:, :], imm_value=NEG).then_inc(s_router, 1)
                dve.wait_ge(s_router, 6 * t + 3)
                dve.sem_inc(s_passed, 1)
                dve.max(out=top_b[:, :], in_=rest_a[:, :]).then_inc(s_router, 1)
                dve.wait_ge(s_router, 6 * t + 4)
                dve.sem_inc(s_passed, 1)
                dve.match_replace(out=rest_b[:, :], in_to_replace=top_b[:, :], in_values=rest_a[:, :], imm_value=NEG).then_inc(s_rest, 1)
                dve.wait_ge(s_exp, 2 * t + 2)
                dve.scalar_tensor_tensor(out=gates[:, :], in0=exp_all[:, :], scalar=1.0, in1=exp_rest[:, :], op0=ALU.mult,
                                         op1=ALU.subtract, accum_out=gate_sum[:, 0:1]).then_inc(s_router, 1)
                dve.wait_ge(s_router, 6 * t + 5)
                if not first:
                    dve.wait_ge(s_out, 16 * t)
                for psum, c0, _, n in reversed(H_PARTS):
                    k0, k1 = c0 // R, (c0 + n) // R
                    dve.tensor_tensor(out=hg[:, c0:c0 + n].rearrange("p (e r) -> p e r", r=R),
                                      in0=psum[:, 0:n].rearrange("p (e r) -> p e r", r=R),
                                      in1=gates[:, k0:k1].unsqueeze(2).to_broadcast([P, k1 - k0, R]), op=ALU.mult).then_inc(s_hg, 1)
                dve.tensor_scalar(gate_sum[:, 1:2], gate_sum[:, 0:1], 1.0 / SCALING, None, ALU.mult).then_inc(s_router, 1)
                if ahead:
                    mask_y(t + 1, 0)
                for n, bank in enumerate((1, 0)):
                    dve.wait_ge(s_ghi, 2 * t + n + 1)
                    dve.tensor_tensor(out=g_lo[:, 4 * bank:4 * bank + 4, :].rearrange("p c n -> p (c n)"), in0=turn_ps[:, bank, :],
                                      in1=g_hi[:, 4 * bank:4 * bank + 4, :].rearrange("p c n -> p (c n)").bitcast(F32),
                                      op=ALU.subtract).then_inc(s_glo, 1)
                if ahead:
                    mask_y(t + 1, 1)
                    low_y(t + 1)
                dve.wait_ge(s_router, 6 * t + 6)
                dve.reciprocal(gate_scale[:, :], gate_sum[:, 1:2]).then_inc(s_scale, 1)
                if chunk:
                    factors(t, views)
                dve.wait_ge(s_scale, t + 1)
                dve.wait_ge(s_x, 16 * t + 16)
                dve.wait_ge(s_down, t + 1)
                dve.scalar_tensor_tensor(out=o_sb[:, :], in0=out_ps[:, :, :].rearrange("p a n -> p (a n)"), scalar=gate_scale[:, :],
                                         in1=x_in[:, :], op0=ALU.mult, op1=ALU.add).then_inc(s_o, 1)
                if chunk:
                    add_skip(t, views)

            step(0, first=True)
            with dve.Fori(1, CHUNKS) as t:
                step(t, chunk=True)
            with dve.Fori(CHUNKS, TILES - 1) as t:
                step(t)
            step(TILES - 1, ahead=False)

        @block.tensor
        def _(pe):
            def build_k(c, buffers):
                wave = buffers[2]
                pe.wait_ge(s_factors, c + 1)
                for h in range(HC):
                    last = pe.matmul(k_ps[:, h * GRID:(h + 1) * GRID], wave[:, 1, h, :], wave[:, 0, h, :], start=True, stop=True)
                last.then_inc(s_kps, 1)

            def conv(i, blocks=range(NC)):
                for d in blocks:
                    n = (NC - d) * B
                    o = conv_ps[i][:, d * B:NC * B]
                    hi, lo = (part[:, i, d * P:(d + 1) * P] for part in (t_hi, t_lo))
                    pe.matmul(o, hi, xt_hi[:, i, 0:n], start=d == 0, stop=False)
                    pe.matmul(o, hi, xt_lo[:, i, 0:n], start=False, stop=False)
                    last = pe.matmul(o, lo, xt_hi[:, i, 0:n], start=False, stop=d == NC - 1)
                return last

            def product(outs, hi, lo, w_hi, w_lo, order, before={}):
                for c in order:
                    if c in before:
                        pe.wait_ge(*before[c])
                    for part, moving in ((hi, w_hi), (hi, w_lo), (lo, w_hi)):
                        for o, c0, n in outs:
                            last = pe.matmul(o, part[:, c, :], moving[:, c, c0:c0 + n], start=c == order[0] and part is hi and moving is w_hi,
                                             stop=c == order[-1] and part is lo)
                return last

            def step(t, ahead=True, first=False, chunk=False):
                pe.wait_ge(s_ylo, t + 1)
                if first:
                    pe.wait_ge(s_wlo, FIRST_B)
                    pe.wait_ge(s_kcopy, 1)
                if not first:
                    pe.wait_ge(s_glo, 2 * t)
                product([(o, c0, n) for o, c0, n, _ in H_PARTS], y_hi, y_lo, a_hi, a_lo, range(NC)).then_inc(s_up, 1)
                if ahead:
                    pe.wait_ge(s_xlo, t + 2)
                    pe.wait_ge(s_tlo, HT * t + HT + 1)
                    pe.wait_ge(s_ym, HT * t + 1)
                    conv(0).then_inc(s_conv, 1)
                    pe.wait_ge(s_tlo, HT * t + HT + 2)
                    pe.wait_ge(s_ym, HT * t + 2)
                    conv(1, range(0, 1))
                if chunk:
                    pe.wait_ge(s_kcopy, t)
                for n, blocks in enumerate(((7, 6), (5, 4), (3,), (2, 1, 0))):
                    if n != 2:
                        pe.wait_ge(s_hg, 3 * t + (1, 2, 2, 3)[n])
                    for c in blocks:
                        last = pe.transpose(turn_ps[:, c // 4, (c % 4) * P:(c % 4 + 1) * P], hg[:, c * P:(c + 1) * P], ident[:, :])
                    if n in (1, 3):
                        last.then_inc(s_turn, 1)
                if ahead:
                    conv(1, range(1, NC)).then_inc(s_conv, 1)
                pe.wait_ge(s_glo, 2 * t + 1)
                if first:
                    pe.wait_ge(s_wlo, len(loads))
                if not first:
                    pe.wait_ge(s_o, t)
                product([(out_ps[:, 0, :], 0, HALF), (out_ps[:, 1, :], HALF, HALF)], g_hi, g_lo, b_hi, b_lo,
                        (4, 5, 6, 7, 0, 1, 2, 3), before={0: (s_glo, 2 * t + 2)}).then_inc(s_down, 1)
                if chunk:
                    build_k(t, views)

            build_k(0, views0)
            pe.wait_ge(s_ident, 2)
            pe.wait_ge(s_xlo, 1)
            for i in range(HT):
                pe.wait_ge(s_tlo, i + 1)
                conv(i).then_inc(s_conv, 1)
            step(0, first=True)
            with pe.Fori(1, CHUNKS) as t:
                step(t, chunk=True)
            with pe.Fori(CHUNKS, TILES - 1) as t:
                step(t)
            step(TILES - 1, ahead=False)


def kernel(x, itok_B_8_3872, L0_cond_log_dt, L0_cond_C, L0_cond_log_A_real, L0_cond_A_imag, L0_cond_D,
           L0_ffn_A, L0_ffn_B, L0_ffn_Wr):
    import numpy as np
    import concourse.bacc as bacc
    from concourse.bass_utils import run_bass_kernel_spmd

    x = np.ascontiguousarray(x)
    xt = x.reshape(B, TILES, HT, NC, P)[..., ::-1].transpose(1, 4, 2, 3, 0).reshape(TILES, P, HT * NC * B)
    c = np.asarray(L0_cond_C)
    parameters = np.empty((2, N, 6, H), x.dtype)
    parameters[:, :, 0] = np.asarray(L0_cond_log_dt)
    parameters[:, :, 1] = np.asarray(L0_cond_log_A_real).T
    parameters[:, :, 2] = np.asarray(L0_cond_A_imag).T
    parameters[:, :, 3] = c[:, :, 0].T
    parameters[:, :, 4] = c[:, :, 1].T
    parameters[:, :, 5] = np.asarray(L0_cond_D)
    parameters = parameters.reshape(P, 6, H)
    arrays = {
        "xt": xt,
        "x": x,
        "length": np.asarray(itok_B_8_3872),
        "parameters": parameters,
        "a_t": np.asarray(L0_ffn_A).reshape(ER, NC, P).transpose(2, 1, 0),
        "b_t": np.asarray(L0_ffn_B).transpose(0, 2, 1).reshape(NE, P, D).transpose(1, 0, 2),
        "wr_t": np.asarray(L0_ffn_Wr).reshape(E, NC, P).transpose(2, 1, 0),
    }
    arrays = {name: np.ascontiguousarray(a) for name, a in arrays.items()}
    nc = bacc.Bacc("TRN2", target_bir_lowering=False, num_devices=1)
    args = {name: nc.dram_tensor(f"in_{name}", a.shape, mybir.dt.from_np(a.dtype), kind="ExternalInput").ap()
            for name, a in arrays.items()}
    out = nc.dram_tensor("out", (B, H, L), F32, kind="ExternalOutput").ap()
    build(nc, out=out, **args)
    result = run_bass_kernel_spmd(nc, [{f"in_{name}": a for name, a in arrays.items()}], core_ids=[0])
    return result.results[0]["out"]
```

```python
from contextlib import ExitStack

import concourse.bass as bass
from concourse import mybir

P = 128
B, H, L = 64, 64, 1024
N = 64
E, R = 64, 16
D = L
ER = E * R
HT = P // B
TILES = H // HT
NC = L // P
NE = ER // P
EW = ER + E
HALF = 512
FAR = 5
NFAR = (NC - FAR) * B
TOPK = 16
SCALING = 32.0 / 16
GRID = 32
HC = 8
CHUNKS = H // HC
AHEAD = ((0, HT), (HT, HC - HT))
K_PARTS = 11
PAD = P - 1
KROW = 1152
NEG = -3.0e38

F32 = mybir.dt.float32
F32R = mybir.dt.float32r
I32 = mybir.dt.int32
BF16 = mybir.dt.bfloat16
ALU = mybir.AluOpType
ACT = mybir.ActivationFunctionType

ROUND = 12582912.0
LOG2E = 1.4426950408889634
LN2_HI, LN2_LO = 0.693359375, -2.12194440e-4
INV_2PI = 0.15915494309189535
TWO_PI_1, TWO_PI_2, TWO_PI_3 = 6.28125, 0.0019350051879882812, 3.0199159819e-07
TWO_PI, PI = 6.2831850, 3.1415925


def build(nc, xt, x, length, parameters, a_t, b_t, wr_t, out):
    k_dram = nc.dram_tensor("k_padded", (H, KROW), F32, kind="Internal")
    k_ap = k_dram.ap()

    def toeplitz(t, i):
        return bass.AP(k_dram, t * (HT * KROW) + i * KROW, [[1, P], [1, L]])

    def rows(array, t):
        return bass.AP(array.tensor, t * (HT * L), [[L, HT], [H * L, B], [1, L]])

    with ExitStack() as ctx:
        def sb(name, shape, dt=F32, where=ctx):
            return where.enter_context(nc.sbuf_tensor(name, shape, dt))

        def ps(name, shape):
            return ctx.enter_context(nc.psum_tensor(name, shape, F32))

        def sem(name):
            return ctx.enter_context(nc.semaphore(name))

        def in_place(name, shape):
            with ExitStack() as loaded:
                arrived = sb(name + "_in", shape, where=loaded)
            return arrived, sb(name + "_lo", shape, F32R)

        a_hi = sb("a_hi", [P, NC, EW], F32R)
        a_in, a_lo = in_place("a", [P, NC, EW])
        t_hi, t_lo = sb("t_hi", [P, HT, L], F32R), sb("t_lo", [P, HT, L], F32R)
        xt_in = sb("xt_in", [P, HT, NC * B])
        xt_parts = sb("xt_parts", [P, 2, HT, NC * B], F32R)
        xt_hi, xt_lo = xt_parts[:, 0], xt_parts[:, 1]
        y_m = sb("y_m", [P, NC, P])
        y_hi, y_lo = sb("y_hi", [P, NC, P], F32R), sb("y_lo", [P, NC, P], F32R)
        x_in = sb("x_in", [P, D])
        g_hi, g_lo = sb("g_hi", [P, NE, P], F32R), sb("g_lo", [P, NE, P], F32R)
        wide = sb("wide", [P, D])
        hg = o_sb = wide
        mask = sb("mask", [P, NC, B], BF16)
        ident = sb("ident", [P, P])
        k_work = sb("k_work", [P, K_PARTS * HC * GRID])
        top_a, top_b = sb("top_a", [P, 8]), sb("top_b", [P, 8])
        score_sb = sb("score_sb", [P, E])
        rest_a, rest_b = sb("rest_a", [P, E]), sb("rest_b", [P, E])
        neg_max, gate_sum, gate_scale = sb("neg_max", [P, 1]), sb("gate_sum", [P, 2]), sb("gate_scale", [P, 1])
        exp_all, exp_rest, gates = sb("exp_all", [P, E]), sb("exp_rest", [P, E]), sb("gates", [P, E])
        rates, turns = sb("rates", [P, 2, H]), sb("turns", [P, 2, H])
        alpha, beta = sb("alpha", [P, H]), sb("beta", [P, H])
        grid, phase, skip = sb("grid", [P, GRID]), sb("phase", [P, 1]), sb("skip", [1, H])

        with ExitStack() as early:
            def scratch(name, shape, dt=F32):
                return sb(name, shape, dt, early)

            par = scratch("par", [P, 6, H])
            len_i, len_f = scratch("len_i", [P, B], I32), scratch("len_f", [P, B])
            pos_i, pos_f = scratch("pos_i", [P, NC], I32), scratch("pos_f", [P, NC])
            grid_i = scratch("grid_i", [P, GRID], I32)
            zeros = scratch("zeros", [H, PAD])
            tmp = [scratch(f"tmp{i}", [P, 2, H]) for i in range(6)]
            pow_i = scratch("pow_i", [P, 2, H], I32)
            tanh_half, sin_half, sin_full = (scratch(n, [P, H]) for n in ("tanh_half", "sin_half", "sin_full"))
            er, ei, fr, fi = (scratch(n, [P, H]) for n in ("er", "ei", "fr", "fi"))
        logs, aim, cc = par[:, 0:2, :], par[:, 2, :], par[:, 3:5, :]
        b_hi = sb("b_hi", [P, NE, D], F32R)
        b_in, b_lo = in_place("b", [P, NE, D])

        def build_views(flat, heads):
            def part(first, n, rows=P):
                v = flat[0:rows, first * heads * GRID:(first + n) * heads * GRID]
                return v.rearrange("p (j h g) -> p j h g", j=n, g=GRID)
            return part(0, 2), part(2, 3), part(5, 3), part(8, 2), part(10, 1, GRID)

        views_ahead = [build_views(k_work[:, K_PARTS * first * GRID:], heads) for first, heads in AHEAD]
        views = build_views(k_work[:, :], HC)

        def ahead_build(n):
            return (n, *AHEAD[n], views_ahead[n])

        def chunk_build(c):
            return (c + 1, c * HC, HC, views)

        conv_ps = [ps(f"conv_ps{i}", [P, NC * B]) for i in range(HT)]
        h_ps = ps("h_ps", [P, 2, HALF])
        turn_ps = ps("turn_ps", [P, 2, HALF])
        out_ps = ps("out_ps", [P, 2, HALF])
        far_ps = [out_ps[:, i, 0:2 * NFAR].rearrange("p (s n) -> p s n", s=2) for i in range(HT)]
        H_PARTS = [(turn_ps[:, 0, 0:EW - 768], 768, EW - 768, ER - 768),
                   (h_ps[:, 1, 0:384], 384, 384, 384), (h_ps[:, 0, 0:384], 0, 384, 384)]
        scores = turn_ps[:, 0, ER - 768:EW - 768]
        k_ps = turn_ps[0:GRID, 1, :]

        s_par, s_len, s_zero, s_xt, s_x, s_out, s_k = (
            sem(n) for n in ("s_par", "s_len", "s_zero", "s_xt", "s_x", "s_out", "s_k"))
        s_t = [sem(f"s_t{i}") for i in range(HT)]
        s_w = [sem(f"s_w{i}") for i in range(1 + NC + NE)]
        s_iota, s_ident, s_calc, s_zeroed = sem("s_iota"), sem("s_ident"), sem("s_calc"), sem("s_zeroed")
        s_mask, s_rates, s_tanh, s_turns, s_sins = (sem(n) for n in ("s_mask", "s_rates", "s_tanh", "s_turns", "s_sins"))
        s_whi, s_wlo, s_wlo_v = sem("s_whi"), sem("s_wlo"), sem("s_wlo_v")
        s_theta, s_whole, s_angle, s_wave, s_mixed, s_factors, s_kps, s_kcopy, s_kdone = (
            sem(n) for n in ("s_theta", "s_whole", "s_angle", "s_wave", "s_mixed", "s_factors", "s_kps", "s_kcopy", "s_kdone"))
        s_thi, s_tlo, s_xhi, s_xlo = sem("s_thi"), sem("s_tlo"), sem("s_xhi"), sem("s_xlo")
        s_far, s_far_lo, s_far_sum, s_unmasked = (sem(n) for n in ("s_far", "s_far_lo", "s_far_sum", "s_unmasked"))
        s_conv, s_ym, s_yhi, s_ylo = sem("s_conv"), sem("s_ym"), sem("s_yhi"), sem("s_ylo")
        s_router, s_negmax, s_rest, s_exp, s_passed, s_scale = (
            sem(n) for n in ("s_router", "s_negmax", "s_rest", "s_exp", "s_passed", "s_scale"))
        s_up, s_hg, s_turn, s_ghi, s_glo, s_down, s_o = (sem(n) for n in ("s_up", "s_hg", "s_turn", "s_ghi", "s_glo", "s_down", "s_o"))

        loads = [(wr_t, a_in[:, :, ER:EW], a_hi[:, :, ER:EW], a_lo[:, :, ER:EW])]
        loads += [(a_t[:, c, :], a_in[:, c, 0:ER], a_hi[:, c, 0:ER], a_lo[:, c, 0:ER]) for c in range(NC)]
        FIRST_B = len(loads)
        loads += [(b_t[:, c, :], b_in[:, c, :], b_hi[:, c, :], b_lo[:, c, :]) for c in range(NE)]

        def on_vector(i):
            return i > FIRST_B and (i - FIRST_B) % 2 == 1

        def low_made(i):
            if on_vector(i):
                return s_wlo_v, sum(on_vector(j) for j in range(i + 1))
            return s_wlo, sum(not on_vector(j) for j in range(i + 1))

        block = ctx.enter_context(nc.Block())

        @block.sync
        def _(sp):
            def load_weights(i):
                source, arrived, _, _ = loads[i]
                sp.dma_start(arrived, source).then_inc(s_w[i], 16)

            def load_toeplitz(t, i):
                sp.dma_start(t_lo[:, i, :].bitcast(F32), toeplitz(t, i)).then_inc(s_t[i], 16)

            def store_k(n, first, heads, buffers):
                sp.wait_ge(s_kdone, n + 1)
                dst = bass.AP(k_dram, first * KROW + PAD, [[GRID, GRID], [KROW, heads], [1, GRID]])
                sp.dma_start(dst, buffers[4][:, 0]).then_inc(s_k, 16)

            sp.dma_start(par[:, :, :], parameters).then_inc(s_par, 16)
            load_weights(0)
            sp.dma_start(xt_in[:, :, :], xt[0, :, :]).then_inc(s_xt, 16)
            for i in range(1, 3):
                load_weights(i)
            sp.dma_start(len_i[:, :], length.partition_broadcast(P)).then_inc(s_len, 16)
            sp.wait_ge(s_zeroed, 1)
            sp.dma_start(k_ap[:, 0:PAD], zeros[:, :]).then_inc(s_zero, 16)
            for i in range(3, FIRST_B - 2):
                load_weights(i)
            store_k(*ahead_build(0))
            load_weights(FIRST_B - 2)
            sp.wait_ge(s_zero, 16)
            sp.wait_ge(s_k, 16)
            for i in range(HT):
                load_toeplitz(0, i)
            load_weights(FIRST_B - 1)
            sp.wait_ge(s_mask, 1)
            for i in range(FIRST_B, FIRST_B + 2):
                load_weights(i)
            sp.wait_ge(s_xlo, 1)
            sp.dma_start(xt_in[:, :, :], xt[1, :, :]).then_inc(s_xt, 16)
            store_k(*ahead_build(1))
            for i in range(FIRST_B + 2, len(loads) - 2):
                load_weights(i)
            sp.wait_ge(s_k, 32)
            for i in range(HT):
                sp.wait_ge(s_conv, i + 1)
                load_toeplitz(1, i)
            for i in range(len(loads) - 2, len(loads)):
                load_weights(i)
            sp.dma_start(x_in[:, :], rows(x, 0)).then_inc(s_x, 16)

            def step(t, ahead2=True, ahead1=True, chunk=False, chunks_done=False, last=False):
                if ahead2:
                    sp.wait_ge(s_xlo, t + 2)
                    sp.dma_start(xt_in[:, :, :], xt[bass.ds(t + 2, 1), :, :].rearrange("t p n -> (t p) n")).then_inc(s_xt, 16)
                    if chunk:
                        sp.wait_ge(s_k, 16 * t + 16)
                    if chunks_done:
                        sp.wait_ge(s_k, 16 * (CHUNKS + 1))
                    for i in range(HT):
                        sp.wait_ge(s_conv, HT * t + HT + i + 1)
                        load_toeplitz(t + 2, i)
                if last:
                    for half in range(2):
                        sp.wait_ge(s_o, 2 * t + half + 1)
                        columns = slice(half * HALF, (half + 1) * HALF)
                        sp.dma_start(rows(out, t)[:, :, columns], o_sb[:, columns]).then_inc(s_out, 16)
                else:
                    sp.wait_ge(s_o, 2 * t + 2)
                    sp.dma_start(rows(out, t), o_sb[:, :]).then_inc(s_out, 16)
                if ahead1:
                    sp.dma_start(x_in[:, :], rows(x, t + 1)).then_inc(s_x, 16)
                if chunk:
                    store_k(*chunk_build(t))

            step(0)
            with sp.Fori(1, CHUNKS) as t:
                step(t, chunk=True)
            with sp.Fori(CHUNKS, TILES - 2) as t:
                step(t, chunks_done=True)
            step(TILES - 2, ahead2=False)
            step(TILES - 1, ahead2=False, ahead1=False, last=True)
            sp.wait_ge(s_out, 16 * (TILES + 1))

        @block.gpsimd
        def _(pool):
            pool.iota(grid_i[:, :], pattern=[[1, GRID]], base=0, channel_multiplier=0).then_inc(s_iota, 1)
            pool.iota(pos_i[:, :], pattern=[[P, NC]], base=0, channel_multiplier=1).then_inc(s_iota, 1)
            pool.memset(zeros[:, :], 0.0).then_inc(s_zeroed, 1)
            pool.memset(ident[:, :], 0.0).then_inc(s_ident, 1)
            pool.wait_ge(s_ident, 1)
            pool.affine_select(out=ident[:, :], in_=ident[:, :], compare_op=ALU.not_equal, fill=1.0,
                               base=0, pattern=[[-1, P]], channel_multiplier=1).then_inc(s_ident, 1)
            for i, (_, arrived, hi, lo) in enumerate(loads):
                if not on_vector(i):
                    pool.wait_ge(s_whi, i + 1)
                    pool.tensor_tensor(out=lo, in0=arrived, in1=hi.bitcast(F32), op=ALU.subtract).then_inc(s_wlo, 1)

        @block.scalar
        def _(act):
            def split_weights(i):
                act.wait_ge(s_w[i], 16)
                _, arrived, hi, _ = loads[i]
                act.activation(hi, arrived, ACT.Copy).then_inc(s_whi, 1)

            def waves(n, first, heads, buffers):
                _, _, wave, decay, _ = buffers
                act.wait_ge(s_angle, n + 1)
                act.activation(wave, wave, ACT.Sin, scale=TWO_PI).then_inc(s_wave, 1)
                act.activation(decay, decay, ACT.Exp).then_inc(s_wave, 1)

            def copy_k(n, first, heads, buffers):
                act.wait_ge(s_kps, n + 1)
                act.activation(buffers[4][:, 0].rearrange("a h b -> a (h b)"), k_ps[:, 0:heads * GRID], ACT.Copy).then_inc(s_kcopy, 1)

            def high_t(t, i):
                act.wait_ge(s_t[i], 16 * t + 16)
                act.activation(t_hi[:, i, :], t_lo[:, i, :].bitcast(F32), ACT.Copy).then_inc(s_thi, 1)

            def far_low(t, i):
                act.wait_ge(s_far, HT * t + i + 1)
                act.activation(y_m[:, FAR:NC, i * B:(i + 1) * B], far_ps[i][:, 1, :].rearrange("p (c b) -> p c b", b=B),
                               ACT.Copy).then_inc(s_far_lo, 1)

            def high_y(t, i):
                act.wait_ge(s_ym, HT * t + i + 1)
                act.activation(y_hi[:, :, i * B:(i + 1) * B], y_m[:, :, i * B:(i + 1) * B], ACT.Copy).then_inc(s_yhi, 1)

            split_weights(0)
            act.wait_ge(s_xt, 16)
            act.activation(xt_hi, xt_in[:, :, :], ACT.Copy).then_inc(s_xhi, 1)
            split_weights(1)
            act.wait_ge(s_rates, 1)
            act.activation(tanh_half[:, :], rates[:, 0, :], ACT.Tanh, scale=0.5).then_inc(s_tanh, 1)
            act.wait_ge(s_turns, 1)
            act.activation(sin_half[:, :], turns[:, 0, :], ACT.Sin, scale=PI).then_inc(s_sins, 1)
            act.activation(sin_full[:, :], turns[:, 0, :], ACT.Sin, scale=TWO_PI).then_inc(s_sins, 1)
            split_weights(2)
            waves(*ahead_build(0))
            for i in range(3, 6):
                split_weights(i)
            copy_k(*ahead_build(0))
            split_weights(6)
            waves(*ahead_build(1))
            split_weights(7)
            for i in range(HT):
                high_t(0, i)
            split_weights(FIRST_B - 1)
            copy_k(*ahead_build(1))
            far_low(0, 0)
            split_weights(FIRST_B)
            high_y(0, 0)
            far_low(0, 1)
            split_weights(FIRST_B + 1)
            high_y(0, 1)
            for i in range(FIRST_B + 2, len(loads) - 2):
                split_weights(i)

            def step(t, ahead=True, first=False, chunk=False):
                if ahead:
                    act.wait_ge(s_conv, HT * t + HT)
                    act.wait_ge(s_xt, 16 * t + 32)
                    act.activation(xt_hi, xt_in[:, :, :], ACT.Copy).then_inc(s_xhi, 1)
                    for i in range(HT):
                        high_t(t + 1, i)
                if first:
                    for i in range(len(loads) - 2, len(loads)):
                        split_weights(i)
                act.wait_ge(s_negmax, t + 1)
                act.activation(exp_all[:, :], score_sb[:, :], ACT.Exp, bias=neg_max[:, :]).then_inc(s_exp, 1)
                act.wait_ge(s_rest, t + 1)
                act.activation(exp_rest[:, :], rest_b[:, :], ACT.Exp, bias=neg_max[:, :]).then_inc(s_exp, 1)
                if ahead:
                    for i in range(HT):
                        far_low(t + 1, i)
                for n, bank in enumerate((1, 0)):
                    act.wait_ge(s_turn, 2 * t + n + 1)
                    act.activation(g_hi[:, 4 * bank:4 * bank + 4, :].rearrange("p c n -> p (c n)"), turn_ps[:, bank, :],
                                   ACT.Copy).then_inc(s_ghi, 1)
                if ahead:
                    for i in range(HT):
                        high_y(t + 1, i)
                if chunk:
                    waves(*chunk_build(t))
                    act.wait_ge(s_k, 16 * t + 16)
                    copy_k(*chunk_build(t))

            step(0, first=True)
            with act.Fori(1, CHUNKS) as t:
                step(t, chunk=True)
            with act.Fori(CHUNKS, TILES - 1) as t:
                step(t)
            step(TILES - 1, ahead=False)

        @block.vector
        def _(dve):
            calc = [0]

            def link(ins):
                calc[0] += 1
                ins.then_inc(s_calc, 1)
                dve.wait_ge(s_calc, calc[0])

            def exp_parts(v):
                k, r, q = (tmp[i][:, :, :] for i in range(3))
                link(dve.tensor_scalar(r, v, -87.0, 88.0, ALU.max, ALU.min))
                link(dve.tensor_scalar(k, r, LOG2E, ROUND, ALU.mult, ALU.add))
                link(dve.tensor_scalar(k, k, ROUND, None, ALU.subtract))
                link(dve.scalar_tensor_tensor(out=r, in0=k, scalar=-LN2_HI, in1=r, op0=ALU.mult, op1=ALU.add))
                link(dve.scalar_tensor_tensor(out=r, in0=k, scalar=-LN2_LO, in1=r, op0=ALU.mult, op1=ALU.add))
                dve.tensor_scalar(pow_i[:, :, :], k, 8388608.0, 127.0 * 8388608.0, ALU.mult, ALU.add)
                link(dve.tensor_scalar(q, r, 1.0 / 5040, 1.0 / 720, ALU.mult, ALU.add))
                link(dve.tensor_tensor(out=q, in0=q, in1=r, op=ALU.mult))
                for coefficient in (1.0 / 120, 1.0 / 24, 1.0 / 6, 0.5, 1.0):
                    link(dve.scalar_tensor_tensor(out=q, in0=q, scalar=coefficient, in1=r, op0=ALU.add, op1=ALU.mult))
                return pow_i[:, :, :].bitcast(F32), q

            def angles(n, first, heads, buffers):
                theta, whole, wave, decay, _ = buffers
                span = bass.ds(first, heads)
                full = [P, 2, heads, GRID]
                g_b = grid[:, :].unsqueeze(1).unsqueeze(1).to_broadcast(full)
                dve.tensor_tensor(out=theta, in0=turns[:, :, span].unsqueeze(3).to_broadcast(full), in1=g_b,
                                  op=ALU.mult).then_inc(s_theta, 1)
                dve.tensor_tensor(out=decay, in0=rates[:, :, span].unsqueeze(3).to_broadcast(full), in1=g_b, op=ALU.mult)
                dve.wait_ge(s_theta, n + 1)
                dve.tensor_scalar(wave[:, 0], theta[:, 0], phase[:, :], None, ALU.add)
                dve.tensor_scalar(wave[:, 1], theta[:, 1], 0.25, None, ALU.add)
                dve.tensor_scalar(whole[:, 2], theta[:, 1], ROUND, ROUND, ALU.add, ALU.subtract).then_inc(s_whole, 1)
                dve.wait_ge(s_whole, 2 * n + 1)
                dve.tensor_scalar(whole[:, 0:2], wave[:, 0:2], ROUND, ROUND, ALU.add, ALU.subtract).then_inc(s_whole, 1)
                dve.tensor_tensor(out=wave[:, 2], in0=theta[:, 1], in1=whole[:, 2], op=ALU.subtract)
                dve.wait_ge(s_whole, 2 * n + 2)
                dve.tensor_tensor(out=wave[:, 0:2], in0=wave[:, 0:2], in1=whole[:, 0:2], op=ALU.subtract).then_inc(s_angle, 1)

            def factors(n, first, heads, buffers):
                _, _, wave, decay, _ = buffers
                span = bass.ds(first, heads)
                dve.wait_ge(s_wave, 2 * n + 2)
                al = alpha[:, span].unsqueeze(2).to_broadcast([P, heads, GRID])
                be = beta[:, span].unsqueeze(2).to_broadcast([P, heads, GRID])
                dve.tensor_tensor(out=wave[:, 1], in0=wave[:, 1], in1=al, op=ALU.mult)
                dve.tensor_tensor(out=wave[:, 2], in0=wave[:, 2], in1=be, op=ALU.mult).then_inc(s_mixed, 1)
                dve.tensor_tensor(out=wave[:, 0], in0=wave[:, 0], in1=decay[:, 0], op=ALU.mult)
                dve.wait_ge(s_mixed, 2 * n + 1)
                dve.tensor_tensor(out=wave[:, 1], in0=wave[:, 1], in1=wave[:, 2], op=ALU.add).then_inc(s_mixed, 1)
                dve.wait_ge(s_mixed, 2 * n + 2)
                dve.tensor_tensor(out=wave[:, 1], in0=wave[:, 1], in1=decay[:, 1], op=ALU.mult).then_inc(s_factors, 1)

            def add_skip(n, first, heads, buffers):
                span = bass.ds(first, heads)
                dve.wait_ge(s_kcopy, n + 1)
                at_zero = buffers[4][0:1, 0, :, 0]
                dve.tensor_tensor(out=at_zero, in0=at_zero, in1=skip[:, span], op=ALU.add).then_inc(s_kdone, 1)

            def low_t(t, i):
                dve.wait_ge(s_thi, HT * t + i + 1)
                dve.tensor_tensor(out=t_lo[:, i, :], in0=t_lo[:, i, :].bitcast(F32), in1=t_hi[:, i, :].bitcast(F32),
                                  op=ALU.subtract).then_inc(s_tlo, 1)

            def low_x(t):
                dve.wait_ge(s_xhi, t + 1)
                dve.tensor_tensor(out=xt_lo, in0=xt_in[:, :, :], in1=xt_hi.bitcast(F32),
                                  op=ALU.subtract).then_inc(s_xlo, 1)

            def add_far(t, i):
                far = y_m[:, FAR:NC, i * B:(i + 1) * B]
                dve.wait_ge(s_far_lo, HT * t + i + 1)
                dve.tensor_tensor(out=far, in0=far_ps[i][:, 0, :].rearrange("p (c b) -> p c b", b=B), in1=far,
                                  op=ALU.add).then_inc(s_far_sum, 1)

            def mask_y(t, i):
                near, far = y_m[:, 0:FAR, i * B:(i + 1) * B], y_m[:, FAR:NC, i * B:(i + 1) * B]
                conv = conv_ps[i][:, :].rearrange("p (c b) -> p c b", b=B)
                dve.wait_ge(s_far_sum, HT * t + i + 1)
                dve.wait_ge(s_conv, HT * t + i + 1)
                dve.tensor_tensor(out=far, in0=conv[:, FAR:NC], in1=far, op=ALU.add).then_inc(s_unmasked, 1)
                dve.tensor_tensor(out=near, in0=conv[:, 0:FAR], in1=mask[:, 0:FAR], op=ALU.mult)
                dve.wait_ge(s_unmasked, HT * t + i + 1)
                dve.tensor_tensor(out=far, in0=far, in1=mask[:, FAR:NC], op=ALU.mult).then_inc(s_ym, 1)

            def low_y(t, i):
                head = slice(i * B, (i + 1) * B)
                dve.wait_ge(s_yhi, HT * t + i + 1)
                dve.tensor_tensor(out=y_lo[:, :, head], in0=y_m[:, :, head], in1=y_hi[:, :, head].bitcast(F32),
                                  op=ALU.subtract).then_inc(s_ylo, 1)

            dve.memset(phase[0:N, :], 0.25)
            dve.memset(phase[N:P, :], 0.0)
            dve.wait_ge(s_iota, 2)
            dve.tensor_copy(pos_f[:, :], pos_i[:, :])
            dve.tensor_copy(grid[:, :], grid_i[:, :])
            dve.wait_ge(s_par, 16)
            dve.tensor_copy(skip[:, :], par[0:1, 5, :])

            s, q = exp_parts(logs)
            dt_a = tmp[4]
            link(dve.scalar_tensor_tensor(out=dt_a[:, :, :], in0=q, scalar=1.0, in1=s, op0=ALU.add, op1=ALU.mult))
            dt, a = dt_a[:, 0, :], dt_a[:, 1, :]
            im, kk = tmp[5][:, 0, :], tmp[5][:, 1, :]
            dve.scalar_tensor_tensor(out=rates[:, 0, :], in0=a, scalar=-1.0, in1=dt, op0=ALU.mult, op1=ALU.mult).then_inc(s_rates, 1)
            link(dve.tensor_tensor(out=im, in0=aim, in1=dt, op=ALU.mult))
            link(dve.tensor_scalar(kk, im, INV_2PI, ROUND, ALU.mult, ALU.add))
            link(dve.tensor_scalar(kk, kk, ROUND, None, ALU.subtract))
            for part in (TWO_PI_1, TWO_PI_2, TWO_PI_3):
                link(dve.scalar_tensor_tensor(out=im, in0=kk, scalar=-part, in1=im, op0=ALU.mult, op1=ALU.add))
            dve.tensor_scalar(turns[:, 0, :], im, INV_2PI, None, ALU.mult).then_inc(s_turns, 1)
            dve.tensor_scalar(rates[:, 1, :], rates[:, 0, :], float(GRID), None, ALU.mult)
            dve.wait_ge(s_turns, 1)
            link(dve.tensor_scalar(im, turns[:, 0, :], float(GRID), None, ALU.mult))
            link(dve.tensor_scalar(kk, im, ROUND, ROUND, ALU.add, ALU.subtract))
            link(dve.tensor_tensor(out=turns[:, 1, :], in0=im, in1=kk, op=ALU.subtract))
            angles(*ahead_build(0))

            em1 = tmp[2][:, 0, :]
            dve.wait_ge(s_tanh, 1)
            link(dve.tensor_scalar(em1, tanh_half[:, :], -0.5, 0.5, ALU.mult, ALU.add))
            link(dve.reciprocal(em1, em1))
            link(dve.tensor_tensor(out=em1, in0=em1, in1=tanh_half[:, :], op=ALU.mult))
            dve.wait_ge(s_sins, 2)
            cm1, den = tmp[0][:, 0, :], tmp[1][:, 0, :]
            u, v = tmp[0][:, 1, :], tmp[1][:, 1, :]
            dve.tensor_tensor(out=u, in0=a, in1=a, op=ALU.mult)
            dve.tensor_tensor(out=v, in0=aim, in1=aim, op=ALU.mult)
            link(dve.scalar_tensor_tensor(out=cm1, in0=sin_half[:, :], scalar=-2.0, in1=sin_half[:, :], op0=ALU.mult, op1=ALU.mult))
            dve.scalar_tensor_tensor(out=ei[:, :], in0=em1, scalar=1.0, in1=sin_full[:, :], op0=ALU.add, op1=ALU.mult)
            dve.tensor_tensor(out=den, in0=u, in1=v, op=ALU.add)
            link(dve.scalar_tensor_tensor(out=er[:, :], in0=cm1, scalar=1.0, in1=em1, op0=ALU.add, op1=ALU.mult))
            dve.reciprocal(den, den)
            link(dve.tensor_tensor(out=er[:, :], in0=er[:, :], in1=cm1, op=ALU.add))
            dve.tensor_tensor(out=u, in0=a, in1=er[:, :], op=ALU.mult)
            link(dve.tensor_tensor(out=v, in0=aim, in1=ei[:, :], op=ALU.mult))
            link(dve.tensor_tensor(out=fr[:, :], in0=v, in1=u, op=ALU.subtract))
            dve.tensor_tensor(out=u, in0=a, in1=ei[:, :], op=ALU.mult)
            link(dve.tensor_tensor(out=v, in0=aim, in1=er[:, :], op=ALU.mult))
            link(dve.scalar_tensor_tensor(out=fi[:, :], in0=u, scalar=-1.0, in1=v, op0=ALU.mult, op1=ALU.subtract))
            dve.tensor_tensor(out=fr[:, :], in0=fr[:, :], in1=den, op=ALU.mult)
            link(dve.tensor_tensor(out=fi[:, :], in0=fi[:, :], in1=den, op=ALU.mult))
            c_re, c_im = cc[:, 0, :], cc[:, 1, :]
            dve.tensor_tensor(out=tmp[0][:, 0, :], in0=c_re, in1=fr[:, :], op=ALU.mult)
            dve.tensor_tensor(out=tmp[0][:, 1, :], in0=c_im, in1=fi[:, :], op=ALU.mult)
            dve.tensor_tensor(out=tmp[1][:, 0, :], in0=c_re, in1=fi[:, :], op=ALU.mult)
            link(dve.tensor_tensor(out=tmp[1][:, 1, :], in0=c_im, in1=fr[:, :], op=ALU.mult))
            dve.tensor_tensor(out=er[:, :], in0=tmp[0][:, 0, :], in1=tmp[0][:, 1, :], op=ALU.subtract)
            link(dve.tensor_tensor(out=ei[:, :], in0=tmp[1][:, 0, :], in1=tmp[1][:, 1, :], op=ALU.add))
            dve.tensor_scalar(alpha[0:N, :], er[0:N, :], 2.0, None, ALU.mult)
            dve.tensor_scalar(alpha[N:P, :], ei[N:P, :], -2.0, None, ALU.mult)
            dve.tensor_scalar(beta[0:N, :], ei[0:N, :], -2.0, None, ALU.mult)
            link(dve.tensor_scalar(beta[N:P, :], er[N:P, :], -2.0, None, ALU.mult))
            factors(*ahead_build(0))
            add_skip(*ahead_build(0))
            angles(*ahead_build(1))
            low_x(0)
            dve.wait_ge(s_len, 16)
            link(dve.tensor_copy(len_f[:, :], len_i[:, :]))
            dve.tensor_tensor(out=mask[:, :, :], in0=pos_f[:, :].unsqueeze(2).to_broadcast([P, NC, B]),
                              in1=len_f[:, :].unsqueeze(1).to_broadcast([P, NC, B]), op=ALU.is_lt).then_inc(s_mask, 1)

            def low_weights(i):
                dve.wait_ge(s_whi, i + 1)
                _, arrived, hi, lo = loads[i]
                dve.tensor_tensor(out=lo, in0=arrived, in1=hi.bitcast(F32), op=ALU.subtract).then_inc(s_wlo_v, 1)

            odd = [i for i in range(len(loads)) if on_vector(i)]
            low_t(0, 0)
            factors(*ahead_build(1))
            low_t(0, 1)
            add_skip(*ahead_build(1))
            for i in range(HT):
                add_far(0, i)
                mask_y(0, i)
                low_y(0, i)
            for i in odd[:-1]:
                low_weights(i)

            def step(t, ahead=True, first=False, chunk=False):
                if ahead:
                    low_x(t + 1)
                    for i in range(HT):
                        low_t(t + 1, i)
                if first:
                    low_weights(odd[-1])
                if chunk:
                    dve.wait_ge(s_kps, t + 1)
                    angles(*chunk_build(t))
                dve.wait_ge(s_up, 3 * t + 1)
                dve.tensor_copy(score_sb[:, :], scores).then_inc(s_router, 1)
                dve.max(out=top_a[:, :], in_=scores).then_inc(s_router, 1)
                dve.wait_ge(s_router, 6 * t + 2)
                dve.tensor_scalar(neg_max[:, :], top_a[:, 0:1], -1.0, None, ALU.mult).then_inc(s_negmax, 1)
                dve.match_replace(out=rest_a[:, :], in_to_replace=top_a[:, :], in_values=score_sb[:, :], imm_value=NEG).then_inc(s_router, 1)
                dve.wait_ge(s_router, 6 * t + 3)
                dve.sem_inc(s_passed, 1)
                dve.max(out=top_b[:, :], in_=rest_a[:, :]).then_inc(s_router, 1)
                dve.wait_ge(s_router, 6 * t + 4)
                dve.sem_inc(s_passed, 1)
                dve.match_replace(out=rest_b[:, :], in_to_replace=top_b[:, :], in_values=rest_a[:, :], imm_value=NEG).then_inc(s_rest, 1)
                dve.wait_ge(s_exp, 2 * t + 2)
                dve.scalar_tensor_tensor(out=gates[:, :], in0=exp_all[:, :], scalar=1.0, in1=exp_rest[:, :], op0=ALU.mult,
                                         op1=ALU.subtract, accum_out=gate_sum[:, 0:1]).then_inc(s_router, 1)
                dve.wait_ge(s_router, 6 * t + 5)
                if not first:
                    dve.wait_ge(s_out, 16 * t)
                for part, (psum, c0, _, n) in enumerate(H_PARTS):
                    if part:
                        dve.wait_ge(s_up, 3 * t + part + 1)
                    k0, k1 = c0 // R, (c0 + n) // R
                    dve.tensor_tensor(out=hg[:, c0:c0 + n].rearrange("p (e r) -> p e r", r=R),
                                      in0=psum[:, 0:n].rearrange("p (e r) -> p e r", r=R),
                                      in1=gates[:, k0:k1].unsqueeze(2).to_broadcast([P, k1 - k0, R]), op=ALU.mult).then_inc(s_hg, 1)
                dve.tensor_scalar(gate_sum[:, 1:2], gate_sum[:, 0:1], 1.0 / SCALING, None, ALU.mult).then_inc(s_router, 1)
                if ahead:
                    for i in range(HT):
                        add_far(t + 1, i)
                    mask_y(t + 1, 0)
                for n, bank in enumerate((1, 0)):
                    dve.wait_ge(s_ghi, 2 * t + n + 1)
                    dve.tensor_tensor(out=g_lo[:, 4 * bank:4 * bank + 4, :].rearrange("p c n -> p (c n)"), in0=turn_ps[:, bank, :],
                                      in1=g_hi[:, 4 * bank:4 * bank + 4, :].rearrange("p c n -> p (c n)").bitcast(F32),
                                      op=ALU.subtract).then_inc(s_glo, 1)
                if ahead:
                    low_y(t + 1, 0)
                    mask_y(t + 1, 1)
                    low_y(t + 1, 1)
                dve.wait_ge(s_router, 6 * t + 6)
                dve.reciprocal(gate_scale[:, :], gate_sum[:, 1:2]).then_inc(s_scale, 1)
                if chunk:
                    factors(*chunk_build(t))
                dve.wait_ge(s_scale, t + 1)
                dve.wait_ge(s_x, 16 * t + 16)
                for half in range(2):
                    columns = slice(half * HALF, (half + 1) * HALF)
                    dve.wait_ge(s_down, 2 * t + half + 1)
                    dve.scalar_tensor_tensor(out=o_sb[:, columns], in0=out_ps[:, half, :], scalar=gate_scale[:, :],
                                             in1=x_in[:, columns], op0=ALU.mult, op1=ALU.add).then_inc(s_o, 1)
                if chunk:
                    add_skip(*chunk_build(t))

            step(0, first=True)
            with dve.Fori(1, CHUNKS) as t:
                step(t, chunk=True)
            with dve.Fori(CHUNKS, TILES - 1) as t:
                step(t)
            step(TILES - 1, ahead=False)

        @block.tensor
        def _(pe):
            def build_k(n, first, heads, buffers):
                wave = buffers[2]
                pe.wait_ge(s_factors, n + 1)
                for h in range(heads):
                    last = pe.matmul(k_ps[:, h * GRID:(h + 1) * GRID], wave[:, 1, h, :], wave[:, 0, h, :], start=True, stop=True)
                last.then_inc(s_kps, 1)

            def conv_far(i):
                for d in range(FAR, NC):
                    n = (NC - d) * B
                    last = pe.matmul(far_ps[i][:, :, (d - FAR) * B:NFAR], t_hi[:, i, d * P:(d + 1) * P], xt_parts[:, :, i, 0:n],
                                     start=d == FAR, stop=d == NC - 1)
                last.then_inc(s_far, 1)

            def conv_high(i, blocks=range(FAR)):
                for d in blocks:
                    n = (NC - d) * B
                    block_d = t_hi[:, i, d * P:(d + 1) * P]
                    pe.matmul(conv_ps[i][:, d * B:NC * B], block_d, xt_hi[:, i, 0:n], start=d == 0, stop=False)
                    pe.matmul(conv_ps[i][:, d * B:NC * B], block_d, xt_lo[:, i, 0:n], start=False, stop=False)

            def conv_low(i):
                for d in range(NC):
                    last = pe.matmul(conv_ps[i][:, d * B:NC * B], t_lo[:, i, d * P:(d + 1) * P], xt_hi[:, i, 0:(NC - d) * B],
                                     start=False, stop=d == NC - 1)
                last.then_inc(s_conv, 1)

            def product_high(o, hi, w_hi, w_lo, columns, order, first=False):
                for c in order:
                    for moving in (w_hi, w_lo):
                        pe.matmul(o, hi[:, c, :], moving[:, c, columns], start=first and c == order[0] and moving is w_hi, stop=False)

            def product_low(o, lo, w_hi, columns, order):
                for c in order:
                    last = pe.matmul(o, lo[:, c, :], w_hi[:, c, columns], start=False, stop=c == order[-1])
                return last

            def step(t, ahead=True, first=False, chunk=False):
                pe.wait_ge(s_yhi, HT * t + HT)
                if first:
                    pe.wait_ge(*low_made(FIRST_B - 1))
                    pe.wait_ge(s_kcopy, 2)
                if not first:
                    pe.wait_ge(s_glo, 2 * t)
                for part, (o, c0, n, _) in enumerate(H_PARTS):
                    product_high(o, y_hi, a_hi, a_lo, slice(c0, c0 + n), range(NC), first=True)
                    if part == 0:
                        pe.wait_ge(s_ylo, HT * t + HT)
                    product_low(o, y_lo, a_hi, slice(c0, c0 + n), range(NC)).then_inc(s_up, 1)
                if ahead:
                    pe.wait_ge(s_xlo, t + 2)
                    pe.wait_ge(s_thi, HT * t + HT + 1)
                    if not first:
                        pe.wait_ge(s_o, 2 * t)
                    conv_far(0)
                    pe.wait_ge(s_ym, HT * t + 1)
                    conv_high(0)
                    pe.wait_ge(s_tlo, HT * t + HT + 1)
                    conv_low(0)
                    pe.wait_ge(s_thi, HT * t + HT + 2)
                    conv_far(1)
                    pe.wait_ge(s_ym, HT * t + 2)
                    conv_high(1, range(0, 1))
                if chunk:
                    pe.wait_ge(s_kcopy, t + 1)
                for n, blocks in enumerate(((7, 6), (5, 4), (3,), (2, 1, 0))):
                    if n != 2:
                        pe.wait_ge(s_hg, 3 * t + (1, 2, 2, 3)[n])
                    for c in blocks:
                        last = pe.transpose(turn_ps[:, c // 4, (c % 4) * P:(c % 4 + 1) * P], hg[:, c * P:(c + 1) * P], ident[:, :])
                    if n in (1, 3):
                        last.then_inc(s_turn, 1)
                if ahead:
                    conv_high(1, range(1, FAR))
                    pe.wait_ge(s_tlo, HT * t + HT + 2)
                    conv_low(1)
                def down_high(half, order, first=False):
                    product_high(out_ps[:, half, :], g_hi, b_hi, b_lo, slice(half * HALF, (half + 1) * HALF), order, first)

                def down_low(half):
                    product_low(out_ps[:, half, :], g_lo, b_hi, slice(half * HALF, (half + 1) * HALF), (4, 5, 6, 7, 0, 1, 2, 3)).then_inc(s_down, 1)

                pe.wait_ge(s_ghi, 2 * t + 1)
                if first:
                    for last in (-2, -1):
                        pe.wait_ge(*low_made(len(loads) + last))
                if ahead:
                    pe.wait_ge(s_far_sum, HT * t + 2 * HT)
                else:
                    pe.wait_ge(s_o, 2 * t)
                for half in range(2):
                    down_high(half, (4, 5, 6, 7), first=True)
                pe.wait_ge(s_ghi, 2 * t + 2)
                down_high(0, (0, 1, 2, 3))
                pe.wait_ge(s_glo, 2 * t + 2)
                down_low(0)
                down_high(1, (0, 1, 2, 3))
                down_low(1)
                if chunk:
                    build_k(*chunk_build(t))

            build_k(*ahead_build(0))
            pe.wait_ge(s_ident, 2)
            pe.wait_ge(s_xlo, 1)
            for i in range(HT):
                pe.wait_ge(s_thi, i + 1)
                conv_far(i)
                conv_high(i)
                if i == 0:
                    pe.wait_ge(s_kcopy, 1)
                    build_k(*ahead_build(1))
                pe.wait_ge(s_tlo, i + 1)
                conv_low(i)
            step(0, first=True)
            with pe.Fori(1, CHUNKS) as t:
                step(t, chunk=True)
            with pe.Fori(CHUNKS, TILES - 1) as t:
                step(t)
            step(TILES - 1, ahead=False)


def kernel(x, itok_B_8_3872, L0_cond_log_dt, L0_cond_C, L0_cond_log_A_real, L0_cond_A_imag, L0_cond_D,
           L0_ffn_A, L0_ffn_B, L0_ffn_Wr):
    import numpy as np
    import concourse.bacc as bacc
    from concourse.bass_utils import run_bass_kernel_spmd

    x = np.ascontiguousarray(x)
    xt = x.reshape(B, TILES, HT, NC, P)[..., ::-1].transpose(1, 4, 2, 3, 0).reshape(TILES, P, HT * NC * B)
    c = np.asarray(L0_cond_C)
    parameters = np.empty((2, N, 6, H), x.dtype)
    parameters[:, :, 0] = np.asarray(L0_cond_log_dt)
    parameters[:, :, 1] = np.asarray(L0_cond_log_A_real).T
    parameters[:, :, 2] = np.asarray(L0_cond_A_imag).T
    parameters[:, :, 3] = c[:, :, 0].T
    parameters[:, :, 4] = c[:, :, 1].T
    parameters[:, :, 5] = np.asarray(L0_cond_D)
    parameters = parameters.reshape(P, 6, H)
    arrays = {
        "xt": xt,
        "x": x,
        "length": np.asarray(itok_B_8_3872),
        "parameters": parameters,
        "a_t": np.asarray(L0_ffn_A).reshape(ER, NC, P).transpose(2, 1, 0),
        "b_t": np.asarray(L0_ffn_B).transpose(0, 2, 1).reshape(NE, P, D).transpose(1, 0, 2),
        "wr_t": np.asarray(L0_ffn_Wr).reshape(E, NC, P).transpose(2, 1, 0),
    }
    arrays = {name: np.ascontiguousarray(a) for name, a in arrays.items()}
    nc = bacc.Bacc("TRN2", target_bir_lowering=False, num_devices=1)
    args = {name: nc.dram_tensor(f"in_{name}", a.shape, mybir.dt.from_np(a.dtype), kind="ExternalInput").ap()
            for name, a in arrays.items()}
    out = nc.dram_tensor("out", (B, H, L), F32, kind="ExternalOutput").ap()
    build(nc, out=out, **args)
    result = run_bass_kernel_spmd(nc, [{f"in_{name}": a for name, a in arrays.items()}], core_ids=[0])
    return result.results[0]["out"]
```
